# Optimizing a Trainium2 kernel written in Bass

```python
import numpy as np
import jax
import jax.numpy as jnp

def _softmax(x, axis=-1):
    return jax.nn.softmax(x, axis=axis)

def _gelu(x):
    return jax.nn.gelu(x, approximate=True)

def _silu(x):
    return jax.nn.silu(x)

def _sigmoid(x):
    return jax.nn.sigmoid(x)

def _layernorm(x, axis=-1, eps=1e-05):
    m = jnp.mean(x, axis=axis, keepdims=True)
    v = jnp.var(x, axis=axis, keepdims=True)
    return (x - m) / jnp.sqrt(v + eps)

def _scatter_add(tgt, idx, src, axis=0):
    return tgt.at[idx].add(src)

def _segment_sum(src, seg, n):
    return jax.ops.segment_sum(src, seg, n)
kernel_name = 'mk_dlrm_tower_d1_rec_r8_87a5d5'

def setup_inputs(seed: int=0):
    np.random.seed(seed)
    _w = jnp.asarray

    def _rec_inputs():
        import jax
        import jax.numpy as jnp
        _tk = jax.random.key(seed)
        dense_ctx = jax.random.normal(jax.random.fold_in(_tk, 190), (2048, 16), jnp.float32)
        ids = jnp.stack([jax.random.randint(jax.random.fold_in(_tk, 200 + f), (2048,), 0, v, jnp.int32) for f, v in enumerate([1250, 1250, 1250, 12500, 125000, 1250, 125000, 1000, 1000, 1000, 125000, 1000, 1000, 1250, 1250, 1000, 1250, 1000, 1000, 12500, 1000, 1250, 1000, 1250, 1000, 1000, 12500, 1000, 1000, 1250, 1250, 1250])], axis=1)
        tbl_0 = 0.05 * jax.random.normal(jax.random.fold_in(_tk, 500 + 0), (1250, 64), jnp.float32)
        tbl_1 = 0.05 * jax.random.normal(jax.random.fold_in(_tk, 500 + 1), (1250, 64), jnp.float32)
        tbl_2 = 0.05 * jax.random.normal(jax.random.fold_in(_tk, 500 + 2), (1250, 64), jnp.float32)
        tbl_3 = 0.05 * jax.random.normal(jax.random.fold_in(_tk, 500 + 3), (12500, 64), jnp.float32)
        tbl_4 = 0.05 * jax.random.normal(jax.random.fold_in(_tk, 500 + 4), (125000, 64), jnp.float32)
        tbl_5 = 0.05 * jax.random.normal(jax.random.fold_in(_tk, 500 + 5), (1250, 64), jnp.float32)
        tbl_6 = 0.05 * jax.random.normal(jax.random.fold_in(_tk, 500 + 6), (125000, 64), jnp.float32)
        tbl_7 = 0.05 * jax.random.normal(jax.random.fold_in(_tk, 500 + 7), (1000, 64), jnp.float32)
        tbl_8 = 0.05 * jax.random.normal(jax.random.fold_in(_tk, 500 + 8), (1000, 64), jnp.float32)
        tbl_9 = 0.05 * jax.random.normal(jax.random.fold_in(_tk, 500 + 9), (1000, 64), jnp.float32)
        tbl_10 = 0.05 * jax.random.normal(jax.random.fold_in(_tk, 500 + 10), (125000, 64), jnp.float32)
        tbl_11 = 0.05 * jax.random.normal(jax.random.fold_in(_tk, 500 + 11), (1000, 64), jnp.float32)
        tbl_12 = 0.05 * jax.random.normal(jax.random.fold_in(_tk, 500 + 12), (1000, 64), jnp.float32)
        tbl_13 = 0.05 * jax.random.normal(jax.random.fold_in(_tk, 500 + 13), (1250, 64), jnp.float32)
        tbl_14 = 0.05 * jax.random.normal(jax.random.fold_in(_tk, 500 + 14), (1250, 64), jnp.float32)
        tbl_15 = 0.05 * jax.random.normal(jax.random.fold_in(_tk, 500 + 15), (1000, 64), jnp.float32)
        tbl_16 = 0.05 * jax.random.normal(jax.random.fold_in(_tk, 500 + 16), (1250, 64), jnp.float32)
        tbl_17 = 0.05 * jax.random.normal(jax.random.fold_in(_tk, 500 + 17), (1000, 64), jnp.float32)
        tbl_18 = 0.05 * jax.random.normal(jax.random.fold_in(_tk, 500 + 18), (1000, 64), jnp.float32)
        tbl_19 = 0.05 * jax.random.normal(jax.random.fold_in(_tk, 500 + 19), (12500, 64), jnp.float32)
        tbl_20 = 0.05 * jax.random.normal(jax.random.fold_in(_tk, 500 + 20), (1000, 64), jnp.float32)
        tbl_21 = 0.05 * jax.random.normal(jax.random.fold_in(_tk, 500 + 21), (1250, 64), jnp.float32)
        tbl_22 = 0.05 * jax.random.normal(jax.random.fold_in(_tk, 500 + 22), (1000, 64), jnp.float32)
        tbl_23 = 0.05 * jax.random.normal(jax.random.fold_in(_tk, 500 + 23), (1250, 64), jnp.float32)
        tbl_24 = 0.05 * jax.random.normal(jax.random.fold_in(_tk, 500 + 24), (1000, 64), jnp.float32)
        tbl_25 = 0.05 * jax.random.normal(jax.random.fold_in(_tk, 500 + 25), (1000, 64), jnp.float32)
        tbl_26 = 0.05 * jax.random.normal(jax.random.fold_in(_tk, 500 + 26), (12500, 64), jnp.float32)
        tbl_27 = 0.05 * jax.random.normal(jax.random.fold_in(_tk, 500 + 27), (1000, 64), jnp.float32)
        tbl_28 = 0.05 * jax.random.normal(jax.random.fold_in(_tk, 500 + 28), (1000, 64), jnp.float32)
        tbl_29 = 0.05 * jax.random.normal(jax.random.fold_in(_tk, 500 + 29), (1250, 64), jnp.float32)
        tbl_30 = 0.05 * jax.random.normal(jax.random.fold_in(_tk, 500 + 30), (1250, 64), jnp.float32)
        tbl_31 = 0.05 * jax.random.normal(jax.random.fold_in(_tk, 500 + 31), (1250, 64), jnp.float32)
        _rk = jax.random.fold_in(_tk, 7)
        W_top1 = 0.0441942 * jax.random.normal(jax.random.fold_in(_tk, 801), (512, 512), jnp.float32)
        W_top2 = 0.0441942 * jax.random.normal(jax.random.fold_in(_tk, 802), (512, 256), jnp.float32)
        W_top3 = 0.0625 * jax.random.normal(jax.random.fold_in(_tk, 803), (256, 1), jnp.float32)
        b_top1 = jnp.zeros((512,), jnp.float32)
        b_top2 = jnp.zeros((256,), jnp.float32)
        return (dense_ctx, ids, tbl_0, tbl_1, tbl_2, tbl_3, tbl_4, tbl_5, tbl_6, tbl_7, tbl_8, tbl_9, tbl_10, tbl_11, tbl_12, tbl_13, tbl_14, tbl_15, tbl_16, tbl_17, tbl_18, tbl_19, tbl_20, tbl_21, tbl_22, tbl_23, tbl_24, tbl_25, tbl_26, tbl_27, tbl_28, tbl_29, tbl_30, tbl_31, W_top1, b_top1, W_top2, b_top2, W_top3)
    dense_ctx, ids, tbl_0, tbl_1, tbl_2, tbl_3, tbl_4, tbl_5, tbl_6, tbl_7, tbl_8, tbl_9, tbl_10, tbl_11, tbl_12, tbl_13, tbl_14, tbl_15, tbl_16, tbl_17, tbl_18, tbl_19, tbl_20, tbl_21, tbl_22, tbl_23, tbl_24, tbl_25, tbl_26, tbl_27, tbl_28, tbl_29, tbl_30, tbl_31, W_top1, b_top1, W_top2, b_top2, W_top3 = _rec_inputs()

    def _L0_rec_setup():
        import jax, jax.numpy as jnp
        import numpy as np
        NUM_FIELDS = 32
        key = jax.random.key(seed)
        x = jax.random.normal(key, (2048, NUM_FIELDS, 64), dtype=jnp.float32)
        return {'x': x}
    _L0_rec_all = _L0_rec_setup()
    _L0_rec_in = {k: v for k, v in _L0_rec_all.items() if k in ()}
    del _L0_rec_all
    return {'dense_ctx': dense_ctx, 'ids': ids, 'tbl_0': tbl_0, 'tbl_1': tbl_1, 'tbl_2': tbl_2, 'tbl_3': tbl_3, 'tbl_4': tbl_4, 'tbl_5': tbl_5, 'tbl_6': tbl_6, 'tbl_7': tbl_7, 'tbl_8': tbl_8, 'tbl_9': tbl_9, 'tbl_10': tbl_10, 'tbl_11': tbl_11, 'tbl_12': tbl_12, 'tbl_13': tbl_13, 'tbl_14': tbl_14, 'tbl_15': tbl_15, 'tbl_16': tbl_16, 'tbl_17': tbl_17, 'tbl_18': tbl_18, 'tbl_19': tbl_19, 'tbl_20': tbl_20, 'tbl_21': tbl_21, 'tbl_22': tbl_22, 'tbl_23': tbl_23, 'tbl_24': tbl_24, 'tbl_25': tbl_25, 'tbl_26': tbl_26, 'tbl_27': tbl_27, 'tbl_28': tbl_28, 'tbl_29': tbl_29, 'tbl_30': tbl_30, 'tbl_31': tbl_31, 'W_top1': W_top1, 'b_top1': b_top1, 'W_top2': W_top2, 'b_top2': b_top2, 'W_top3': W_top3}

def reference(dense_ctx, ids, tbl_0, tbl_1, tbl_2, tbl_3, tbl_4, tbl_5, tbl_6, tbl_7, tbl_8, tbl_9, tbl_10, tbl_11, tbl_12, tbl_13, tbl_14, tbl_15, tbl_16, tbl_17, tbl_18, tbl_19, tbl_20, tbl_21, tbl_22, tbl_23, tbl_24, tbl_25, tbl_26, tbl_27, tbl_28, tbl_29, tbl_30, tbl_31, W_top1, b_top1, W_top2, b_top2, W_top3):
    import jax
    import jax.numpy as jnp

    def _L0_rec_ref(x):
        import jax, jax.numpy as jnp
        import numpy as np
        NUM_FIELDS = 32
        n = x.shape[1]
        gram = jnp.einsum('bnd,bmd->bnm', x, x)
        rows, cols = jnp.triu_indices(n, k=1)
        inner_product = gram[:, rows, cols][..., None]
        return inner_product
    e = jnp.stack([tbl_0[ids[:, 0]], tbl_1[ids[:, 1]], tbl_2[ids[:, 2]], tbl_3[ids[:, 3]], tbl_4[ids[:, 4]], tbl_5[ids[:, 5]], tbl_6[ids[:, 6]], tbl_7[ids[:, 7]], tbl_8[ids[:, 8]], tbl_9[ids[:, 9]], tbl_10[ids[:, 10]], tbl_11[ids[:, 11]], tbl_12[ids[:, 12]], tbl_13[ids[:, 13]], tbl_14[ids[:, 14]], tbl_15[ids[:, 15]], tbl_16[ids[:, 16]], tbl_17[ids[:, 17]], tbl_18[ids[:, 18]], tbl_19[ids[:, 19]], tbl_20[ids[:, 20]], tbl_21[ids[:, 21]], tbl_22[ids[:, 22]], tbl_23[ids[:, 23]], tbl_24[ids[:, 24]], tbl_25[ids[:, 25]], tbl_26[ids[:, 26]], tbl_27[ids[:, 27]], tbl_28[ids[:, 28]], tbl_29[ids[:, 29]], tbl_30[ids[:, 30]], tbl_31[ids[:, 31]]], axis=1)
    z = _L0_rec_ref(e)
    z = z.reshape(z.shape[0], -1)
    h = jnp.concatenate([z, dense_ctx], axis=1)
    h = jnp.maximum(h @ W_top1 + b_top1, 0.0)
    h = jnp.maximum(h @ W_top2 + b_top2, 0.0)
    y = h @ W_top3
    return y

_drawn_inputs = setup_inputs


def setup_inputs(seed=0):
    import zlib

    import numpy as np

    out = dict(_drawn_inputs(seed))
    spreads = {'b_top1': (0.0, 0.1), 'b_top2': (0.0, 0.1)}
    factors = {}
    for name, (base, spread) in spreads.items():
        noise = np.random.default_rng([zlib.crc32(name.encode()), seed]).standard_normal(out[name].shape)
        drawn = base * np.exp(spread * noise) if base else spread * noise
        out[name] = jnp.asarray(drawn.astype(out[name].dtype))
    for name, factor in factors.items():
        out[name] = (out[name] * factor).astype(out[name].dtype)
    return out
```

```python
from contextlib import ExitStack

import concourse.bass as bass
from concourse import mybir

F32 = mybir.dt.float32
BF16 = mybir.dt.bfloat16
F16 = mybir.dt.float16
I32 = mybir.dt.int32
ALU = mybir.AluOpType
ACT = mybir.ActivationFunctionType

BATCH, FIELDS, DIM, CTX = 2048, 32, 64, 16
P = 128
UNIT = 2 * P
UNITS = BATCH // UNIT
SELECTED = [7, 8, 9, 11, 12, 15, 17, 18, 20, 22, 24, 25]
GATHERED = [f for f in range(FIELDS) if f not in SELECTED]
N_SEL, N_GAT = len(SELECTED), len(GATHERED)
KROWS = 125
PARTS = 3
RING = 4
PER_BANK = 4
Q = 4
CH = FIELDS // Q
H1, H2 = 512, 256
J1, J2 = H1 // P, H2 // P


def grouped(fields):
    return [fields[i:i + PER_BANK] for i in range(0, len(fields), PER_BANK)]


def runs(fields):
    out, i = [], 0
    while i < len(fields):
        k = i + 1
        step = fields[k] - fields[i] if k < len(fields) else 1
        while k < len(fields) and fields[k] - fields[k - 1] == step:
            k += 1
        out.append((i, fields[i], step, k - i))
        i = k
    return out


SEL_GROUPS, GAT_GROUPS = grouped(SELECTED), grouped(GATHERED)
GROUPS = len(SEL_GROUPS) + len(GAT_GROUPS) + 1


def pair_row(n, m):
    return n * (2 * FIELDS - 1 - n) // 2 + m - n - 1


def dlrm_tower_kernel(nc, dense_ctx, ids, tables, w1, b1, w2, b2, w3, out):
    chunks = [tables[f].shape[0] // KROWS for f in SELECTED]
    first_chunk = [sum(chunks[:i]) for i in range(N_SEL)]
    most = max(chunks)
    stage_chunks = max(sum(chunks[PER_BANK * g:PER_BANK * g + PER_BANK]) for g in range(len(SEL_GROUPS)))

    with ExitStack() as ctx:
        def sb(name, shape, dt):
            return ctx.enter_context(nc.sbuf_tensor(name, shape, dt))

        def psum(name, shape, dt):
            return ctx.enter_context(nc.psum_tensor(name, shape, dt))

        def sem(name):
            return ctx.enter_context(nc.semaphore(name))

        ident = sb("ident", [P, P], F32)
        row_ids = {c: sb(f"row_ids{c}", [P, c], F32) for c in sorted(set(chunks))}
        ids_all = sb("ids_all", [P, BATCH // P, FIELDS], I32)
        ids_sel = sb("ids_sel", [P, BATCH // P, N_SEL], F32)
        ids_t = sb("ids_t", [N_SEL, BATCH], F16)
        ids_unit = [sb(f"ids_unit{b}", [P, 2, FIELDS], I32) for b in range(2)]
        ctx_unit = [sb(f"ctx_unit{b}", [P, 2, 32], F32) for b in range(2)]
        ids_wide = [sb(f"ids_wide{b}", [P, N_SEL, UNIT], F16) for b in range(2)]
        stage = [sb(f"stage{b}", [KROWS, stage_chunks, DIM], F32) for b in range(2)]
        rest = sb("rest", [KROWS, stage_chunks, DIM], F32)
        tabs = sb("tabs", [KROWS, sum(chunks), PARTS, DIM], BF16)
        onehot = [sb(f"onehot{r}", [KROWS, most, UNIT], BF16) for r in range(RING)]
        rows = [sb(f"rows{b}", [P, N_GAT, 2, DIM], F32) for b in range(2)]
        vecs = sb("vecs", [P, P, FIELDS], F32)
        prods = sb("prods", [P, CH, UNIT], F32)
        w1_sb = sb("w1_sb", [P, CH, H1], F32)
        w2_sb = sb("w2_sb", [P, J1, H2], F32)
        w3_sb = sb("w3_sb", [P, J2], F32)
        b1_sb = sb("b1_sb", [P, J1], F32)
        b2_sb = sb("b2_sb", [P, J2], F32)
        h1 = sb("h1", [P, J1, UNIT], F32)
        h2 = sb("h2", [P, J2, UNIT], F32)
        y = [sb(f"y{b}", [1, UNIT], F32) for b in range(2)]

        vecs_ps = psum("vecs_ps", [P, 2, PER_BANK, P], F32)
        prods_ps = psum("prods_ps", [P, 2, 32, FIELDS], F32)
        h1_ps = psum("h1_ps", [P, J1, UNIT], F32)
        h2_ps = prods_ps[:, 0, 0:16, :].rearrange("p i m -> p (i m)").rearrange("p (j s) -> p j s", j=J2)
        y_ps = prods_ps[0:1, 1, 0:8, :].rearrange("p i m -> p (i m)")
        idt_ps = prods_ps[0:N_SEL].rearrange("p h i m -> p (h i m)")

        ids_scratch = nc.dram_tensor("ids_scratch", (N_SEL, BATCH), F16, kind="Internal").ap()

        ids_all_in = sem("ids_all_in")
        ids_in = [sem(f"ids_in{b}") for b in range(2)]
        ctx_in = [sem(f"ctx_in{b}") for b in range(2)]
        wide_in = [sem(f"wide_in{b}") for b in range(2)]
        stage_in = [sem(f"stage_in{b}") for b in range(2)]
        scratch_out = sem("scratch_out")
        w1_in = sem("w1_in")
        w_in = sem("w_in")
        rows_in = [sem(f"rows_in{b}") for b in range(2)]
        y_out = [sem(f"y_out{b}") for b in range(2)]
        ident_zero = sem("ident_zero")
        ident_ready = sem("ident_ready")
        row_ids_ready = sem("row_ids_ready")
        w1_zero = sem("w1_zero")
        ctx_zero = sem("ctx_zero")
        ids_float = sem("ids_float")
        ids_turned = sem("ids_turned")
        ids_t_ready = sem("ids_t_ready")
        split_step = sem("split_step")
        onehot_ready = sem("onehot_ready")
        onehot_used = sem("onehot_used")
        group_full = sem("group_full")
        group_emptied = sem("group_emptied")
        gram_full = sem("gram_full")
        prods_ready = sem("prods_ready")
        h1_full = sem("h1_full")
        h1_ready = sem("h1_ready")
        h2_full = sem("h2_full")
        h2_ready = sem("h2_ready")
        y_full = sem("y_full")
        y_free = sem("y_free")
        y_ready = sem("y_ready")

        passed = {e: sem(f"passed_{e}") for e in ("pe", "pool", "sp")}

        block = ctx.enter_context(nc.Block())
        group_chunks = [(first_chunk[PER_BANK * g], sum(chunks[PER_BANK * g:PER_BANK * g + PER_BANK]))
                        for g in range(len(SEL_GROUPS))]

        @block.sync
        def _(sp):
            def load_unit(n, b):
                sp.dma_start(ids_unit[b][:], ids[bass.ds(n * UNIT, UNIT), :].rearrange("(h p) f -> p h f", p=P))\
                  .then_inc(ids_in[b], 16)
                sp.dma_start(ctx_unit[b][:, :, 0:CTX],
                             dense_ctx[bass.ds(n * UNIT, UNIT), :].rearrange("(h p) f -> p h f", p=P))\
                  .then_inc(ctx_in[b], 16)

            def load_wide(n, b):
                sp.dma_start(ids_wide[b][:], ids_scratch[:, bass.ds(n * UNIT, UNIT)].partition_broadcast(P))\
                  .then_inc(wide_in[b], 16)

            def load_stage(g):
                for i, f in enumerate(SEL_GROUPS[g]):
                    at = first_chunk[PER_BANK * g + i] - group_chunks[g][0]
                    c = chunks[PER_BANK * g + i]
                    sp.dma_start(stage[g % 2][:, at:at + c, :], tables[f].rearrange("(p c) d -> p c d", c=c))\
                      .then_inc(stage_in[g % 2], 16)

            sp.sem_inc(y_free, 2)
            sp.wait_ge(ctx_zero, 2)
            load_unit(0, 0)
            sp.dma_start(ids_all[:], ids.rearrange("(t p) f -> p t f", p=P)).then_inc(ids_all_in, 16)
            load_stage(0)
            load_unit(1, 1)
            load_stage(1)
            sp.wait_ge(ids_t_ready, 1)
            sp.dma_start(ids_scratch, ids_t[:]).then_inc(scratch_out, 16)
            sp.wait_ge(scratch_out, 16)
            load_wide(0, 0)
            load_wide(1, 1)
            for g in range(2, len(SEL_GROUPS)):
                sp.wait_ge(split_step, 4 * (g - 1))
                load_stage(g)
            sp.dma_start(b1_sb[:], b1.rearrange("(c p) -> p c", p=P), allow_slow_non_contiguous=True).then_inc(w_in, 16)
            sp.dma_start(b2_sb[:], b2.rearrange("(c p) -> p c", p=P), allow_slow_non_contiguous=True).then_inc(w_in, 16)
            sp.dma_start(w3_sb[:], w3.rearrange("(c p) a -> p (c a)", p=P), allow_slow_non_contiguous=True).then_inc(w_in, 16)
            sp.dma_start(w2_sb[:], w2.rearrange("(c p) j -> p c j", p=P)).then_inc(w_in, 16)
            sp.wait_ge(w1_zero, 1)
            sp.dma_start(w1_sb[0:CTX, 0, :], w1[FIELDS * (FIELDS - 1) // 2:, :]).then_inc(w1_in, 16)
            for n in range(FIELDS - 1):
                for q in range((n + 1) // CH, Q):
                    m = max(n + 1, CH * q)
                    k = CH * (q + 1) - m
                    sp.dma_start(w1_sb[32 * q + n:32 * q + n + 1, m - CH * q:CH, :],
                                 w1[pair_row(n, m):pair_row(n, m) + k, :].rearrange("(a k) j -> a k j", a=1))\
                      .then_inc(w1_in, 16)

            def step(n, i, b, more):
                if more:
                    sp.wait_ge(rows_in[b], 16 * 2 * N_GAT * (i + 1))
                    sp.sem_inc(passed["sp"], 1)
                    sp.wait_ge(group_full, GROUPS * (n + 1))
                    sp.sem_inc(passed["sp"], 1)
                    load_unit(n + 2, b)
                    sp.wait_ge(onehot_ready, N_SEL * (n + 1))
                    sp.sem_inc(passed["sp"], 1)
                    load_wide(n + 2, b)
                sp.wait_ge(y_ready, n + 2)
                sp.sem_inc(passed["sp"], 1)
                sp.dma_start(out[bass.ds(n * UNIT, UNIT), :].rearrange("s a -> a s"), y[b][:]).then_inc(y_out[b], 16)
                sp.wait_ge(y_out[b], 16 * (i + 1))
                sp.sem_inc(y_free, 1)

            with sp.Fori(0, UNITS // 2 - 1) as i:
                for b in range(2):
                    step(2 * i + b, i, b, True)
            for b in range(2):
                step(UNITS - 2 + b, UNITS // 2 - 1, b, False)

        @block.gpsimd
        def _(pool):
            nc.gpsimd.memset(ident[:], 0.0).then_inc(ident_zero, 1)
            pool.wait_ge(ident_zero, 1)
            nc.gpsimd.affine_select(out=ident[:], in_=ident[:], compare_op=ALU.not_equal, fill=1.0, base=0,
                                    pattern=[[-1, P]], channel_multiplier=1).then_inc(ident_ready, 1)
            for c, t in row_ids.items():
                nc.gpsimd.iota(t[:], pattern=[[1, c]], base=0, channel_multiplier=c,
                               allow_small_or_imprecise_dtypes=True).then_inc(row_ids_ready, 1)
            with pool.Fori(0, UNITS // 2) as i:
                for b in range(2):
                    pool.wait_ge(ids_in[b], 16 * (i + 1))
                    pool.wait_ge(prods_ready, 2 * i + b + 1)
                    pool.sem_inc(passed["pool"], 1)
                    for k, f in enumerate(GATHERED):
                        for h in range(2):
                            nc.gpsimd.indirect_dma_start(
                                out=rows[b][:, k, h, :], out_offset=None, in_=tables[f],
                                in_offset=bass.IndirectOffsetOnAxis(ap=ids_unit[b][:, h, f:f + 1], axis=0))\
                              .then_inc(rows_in[b], 16)

        @block.scalar
        def _(act):
            act.sem_inc(prods_ready, 2)
            act.sem_inc(group_emptied, 2)

            def empty(n, g, b, fields):
                act.wait_ge(group_full, GROUPS * n + g + 1)
                bank = (b * GROUPS + g) % 2
                for at, f, step, count in runs(fields):
                    last = nc.scalar.copy(vecs[:, :, f:f + step * (count - 1) + 1:step].rearrange("p s f -> p f s"),
                                          vecs_ps[:, bank, at:at + count, :])
                last.then_inc(group_emptied, 1)

            def empty_selected(n, b):
                for g, fields in enumerate(SEL_GROUPS):
                    empty(n, g, b, fields)

            def step(n, b, more):
                for g, fields in enumerate(GAT_GROUPS):
                    empty(n, len(SEL_GROUPS) + g, b, fields)
                act.wait_ge(group_full, GROUPS * (n + 1))
                bank = (b * GROUPS + GROUPS - 1) % 2
                nc.scalar.copy(prods[0:32, 0, :], vecs_ps[0:32, bank, 0:2, :].rearrange("p a s -> p (a s)"))\
                  .then_inc(group_emptied, 1)
                act.wait_ge(gram_full, n + 1)
                for s in range(Q):
                    for q in range(Q):
                        c0 = 1 if q == 0 else 0
                        last = nc.scalar.copy(
                            prods[32 * q:32 * q + 32, c0:CH, :].rearrange("p c (h s i) -> p h s i c", h=2, s=Q)[:, :, s],
                            prods_ps[32 * s:32 * s + 32, :, :, CH * q + c0:CH * q + CH])
                last.then_inc(prods_ready, 1)
                if more:
                    empty_selected(n + 1, 1 - b)

            empty_selected(0, 0)
            with act.Fori(0, UNITS // 2 - 1) as i:
                for b in range(2):
                    step(2 * i + b, b, True)
            step(UNITS - 2, 0, True)
            step(UNITS - 1, 1, False)

        @block.vector
        def _(dve):
            for b in range(2):
                nc.vector.memset(ctx_unit[b][:], 0.0).then_inc(ctx_zero, 1)
            nc.vector.memset(w1_sb[:], 0.0).then_inc(w1_zero, 1)
            dve.wait_ge(ids_all_in, 16)
            for at, f, step_, count in runs(SELECTED):
                last = nc.vector.tensor_copy(ids_sel[:, :, at:at + count],
                                             ids_all[:, :, f:f + step_ * (count - 1) + 1:step_])
            last.then_inc(ids_float, 1)

            def split(g):
                c0, k = group_chunks[g]
                dve.wait_ge(stage_in[g % 2], 16 * sum(len(SEL_GROUPS[x]) for x in range(g % 2, g + 1, 2)))
                src, r = stage[g % 2][:, 0:k, :], rest[:, 0:k, :]
                nc.vector.tensor_copy(tabs[:, c0:c0 + k, 0, :], src).then_inc(split_step, 1)
                dve.wait_ge(split_step, 4 * g + 1)
                nc.vector.tensor_tensor(r, src, tabs[:, c0:c0 + k, 0, :], ALU.subtract).then_inc(split_step, 1)
                dve.wait_ge(split_step, 4 * g + 2)
                nc.vector.tensor_copy(tabs[:, c0:c0 + k, 1, :], r).then_inc(split_step, 1)
                dve.wait_ge(split_step, 4 * g + 3)
                nc.vector.tensor_tensor(tabs[:, c0:c0 + k, 2, :], r, tabs[:, c0:c0 + k, 1, :],
                                        ALU.subtract).then_inc(split_step, 1)

            split(0)
            dve.wait_ge(ids_turned, 1)
            nc.vector.tensor_copy(ids_t[:], idt_ps).then_inc(ids_t_ready, 1)
            for g in range(1, len(SEL_GROUPS)):
                split(g)
            dve.wait_ge(row_ids_ready, len(row_ids))

            def one_hots(n, i, b):
                dve.wait_ge(wide_in[b], 16 * (i + 1))
                for k in range(N_SEL):
                    before = k - RING if k >= RING else (N_SEL - 1 - (N_SEL - 1 - k) % RING) - N_SEL
                    dve.wait_ge(onehot_used, N_SEL * (n + 1) + before + 1)
                    for c in range(chunks[k]):
                        last = nc.vector.tensor_scalar(onehot[k % RING][:, c, :], ids_wide[b][0:KROWS, k, :],
                                                       row_ids[chunks[k]][0:KROWS, c:c + 1], None, ALU.is_equal)
                    last.then_inc(onehot_ready, 1)

            def mlp(n, i, b):
                for j in range(J1):
                    if j % 2 == 0:
                        dve.wait_ge(h1_full, 2 * n + j // 2 + 1)
                    nc.vector.tensor_scalar(h1[:, j, :], h1_ps[:, j, :], b1_sb[:, j:j + 1], 0.0, ALU.add,
                                            ALU.max).then_inc(h1_ready, 1)
                dve.wait_ge(h2_full, n + 1)
                for j in range(J2):
                    nc.vector.tensor_scalar(h2[:, j, :], h2_ps[:, j, :], b2_sb[:, j:j + 1], 0.0, ALU.add,
                                            ALU.max).then_inc(h2_ready, 1)
                dve.wait_ge(y_full, n + 1)
                dve.wait_ge(y_free, n + 1)
                nc.vector.tensor_copy(y[b][:], y_ps).then_inc(y_ready, 1)

            dve.sem_inc(y_ready, 1)
            one_hots(0, 0, 0)
            dve.wait_ge(w_in, 16 * 4)
            with dve.Fori(0, UNITS // 2 - 1) as i:
                one_hots(2 * i + 1, i, 1)
                mlp(2 * i, i, 0)
                one_hots(2 * i + 2, i + 1, 0)
                mlp(2 * i + 1, i, 1)
            last_i = UNITS // 2 - 1
            one_hots(UNITS - 1, last_i, 1)
            mlp(UNITS - 2, last_i, 0)
            mlp(UNITS - 1, last_i, 1)

        @block.tensor
        def _(pe):
            pe.sem_inc(onehot_used, N_SEL)

            def start_group(n, g):
                pe.wait_ge(group_emptied, GROUPS * n + g + 1)

            def select(n, b):
                for g, fields in enumerate(SEL_GROUPS):
                    start_group(n, g)
                    bank = (b * GROUPS + g) % 2
                    for at in range(len(fields)):
                        k = PER_BANK * g + at
                        pe.wait_ge(onehot_ready, N_SEL * n + k + 1)
                        for c in range(chunks[k]):
                            for part in range(PARTS):
                                for h in range(2):
                                    last = nc.tensor.matmul(
                                        vecs_ps[DIM * h:DIM * h + DIM, bank, at, :],
                                        tabs[:, first_chunk[k] + c, part, :],
                                        onehot[k % RING][:, c, h * P:h * P + P],
                                        start=(c == 0 and part == 0), stop=(c == chunks[k] - 1 and part == PARTS - 1),
                                        skip_group_check=True)
                        if at < len(fields) - 1:
                            last.then_inc(onehot_used, 1)
                        else:
                            last.then_inc(group_full, 1)
                    pe.wait_ge(group_full, GROUPS * n + g + 1)
                    pe.sem_inc(onehot_used, 1)

            def turn(n, i, b):
                pe.wait_ge(rows_in[b], 16 * 2 * N_GAT * (i + 1))
                for g, fields in enumerate(GAT_GROUPS):
                    start_group(n, len(SEL_GROUPS) + g)
                    bank = (b * GROUPS + len(SEL_GROUPS) + g) % 2
                    for at in range(len(fields)):
                        k = PER_BANK * g + at
                        last = nc.tensor.transpose(vecs_ps[:, bank, at, :],
                                                   rows[b][:, k, :, :].rearrange("p h d -> p (h d)"), ident[:])
                    last.then_inc(group_full, 1)
                start_group(n, GROUPS - 1)
                pe.wait_ge(ctx_in[b], 16 * (i + 1))
                bank = (b * GROUPS + GROUPS - 1) % 2
                for h in range(2):
                    last = nc.tensor.transpose(vecs_ps[0:32, bank, h, :], ctx_unit[b][:, h, :], ident[:])
                last.then_inc(group_full, 1)

            def gram(n):
                pe.wait_ge(group_emptied, GROUPS * (n + 1) + 2)
                pe.wait_ge(y_ready, n + 1)
                pe.sem_inc(passed["pe"], 1)
                for i in range(32):
                    for h in range(2):
                        for s in range(Q):
                            v = vecs[DIM * h:DIM * h + DIM, 32 * s + i, :]
                            last = nc.tensor.matmul(prods_ps[32 * s:32 * s + 32, h, i, :], v, v, start=True, stop=True,
                                                    skip_group_check=True)
                last.then_inc(gram_full, 1)

            def mlp(n):
                pe.wait_ge(prods_ready, n + 3)
                for j in range(J1):
                    for c in range(CH):
                        last = nc.tensor.matmul(h1_ps[:, j, :], w1_sb[:, c, P * j:P * j + P], prods[:, c, :],
                                                start=(c == 0), stop=(c == CH - 1))
                    if j % 2 == 1:
                        last.then_inc(h1_full, 1)
                for j in range(J1):
                    pe.wait_ge(h1_ready, J1 * n + j + 1)
                    for o in range(J2):
                        last = nc.tensor.matmul(h2_ps[:, o, :], w2_sb[:, j, P * o:P * o + P], h1[:, j, :],
                                                start=(j == 0 and o == 0), stop=(j == J1 - 1), skip_group_check=True)
                last.then_inc(h2_full, 1)
                for o in range(J2):
                    pe.wait_ge(h2_ready, J2 * n + o + 1)
                    last = nc.tensor.matmul(y_ps, w3_sb[:, o:o + 1], h2[:, o, :], start=(o == 0), stop=(o == J2 - 1))
                last.then_inc(y_full, 1)

            pe.wait_ge(ident_ready, 1)
            pe.wait_ge(ids_float, 1)
            for t in range(BATCH // P):
                last = nc.tensor.transpose(idt_ps[:, P * t:P * t + P], ids_sel[:, t, :], ident[:])
            last.then_inc(ids_turned, 1)
            pe.wait_ge(split_step, 4 * len(SEL_GROUPS))
            select(0, 0)
            pe.wait_ge(ids_t_ready, 1)
            pe.wait_ge(w1_in, 16 * (1 + sum(Q - (n + 1) // CH for n in range(FIELDS - 1))))
            pe.wait_ge(w_in, 16 * 4)
            with pe.Fori(0, UNITS // 2 - 1) as i:
                for b in range(2):
                    turn(2 * i + b, i, b)
                    gram(2 * i + b)
                    select(2 * i + b + 1, 1 - b)
                    mlp(2 * i + b)
            last_i = UNITS // 2 - 1
            turn(UNITS - 2, last_i, 0)
            gram(UNITS - 2)
            select(UNITS - 1, 1)
            mlp(UNITS - 2)
            turn(UNITS - 1, last_i, 1)
            gram(UNITS - 1)
            mlp(UNITS - 1)


_INS = ["dense_ctx", "ids"] + [f"tbl_{f}" for f in range(FIELDS)] + ["W_top1", "b_top1", "W_top2", "b_top2", "W_top3"]


def kernel(**inputs):
    import numpy as _np
    import concourse.bacc as _bacc
    from concourse import mybir as _mybir
    from concourse.bass_utils import run_bass_kernel_spmd as _run

    nc = _bacc.Bacc("TRN2", target_bir_lowering=False, num_devices=1)
    arrays, args = {}, {}
    for name in _INS:
        a = _np.ascontiguousarray(inputs[name])
        arrays[f"in_{name}_dram"] = a
        args[name] = nc.dram_tensor(f"in_{name}_dram", a.shape, _mybir.dt.from_np(a.dtype), kind="ExternalInput").ap()
    out = nc.dram_tensor("out_0_dram", (BATCH, 1), _mybir.dt.float32, kind="ExternalOutput").ap()
    dlrm_tower_kernel(nc, args["dense_ctx"], args["ids"], [args[f"tbl_{f}"] for f in range(FIELDS)], args["W_top1"],
                      args["b_top1"], args["W_top2"], args["b_top2"], args["W_top3"], out)
    r = _run(nc, [arrays], core_ids=[0])
    return r.results[0]["out_0_dram"]
```

```python
from contextlib import ExitStack

import concourse.bass as bass
from concourse import mybir

F32 = mybir.dt.float32
F32R = mybir.dt.float32r
F16 = mybir.dt.float16
I32 = mybir.dt.int32
ALU = mybir.AluOpType

BATCH, FIELDS, DIM, CTX = 2048, 32, 64, 16
P = 128
UNIT = 2 * P
UNITS = BATCH // UNIT
SELECTED = [7, 8, 9, 11, 12, 15, 17, 18, 20, 22, 24, 25]
GATHERED = [f for f in range(FIELDS) if f not in SELECTED]
N_SEL, N_GAT = len(SELECTED), len(GATHERED)
KROWS = 125
PARTS = 2
RING = 4
STAGED = 4
STAGES = N_SEL // STAGED
SEL_BANK = 2
GAT_BANK = 4
Q = 4
CH = FIELDS // Q
ROUNDS = 2
PER_ROUND = 32 // ROUNDS
H1, H2 = 512, 256
J1, J2 = H1 // P, H2 // P


def grouped(fields, size):
    return [fields[i:i + size] for i in range(0, len(fields), size)]


def runs(fields):
    out, i = [], 0
    while i < len(fields):
        k = i + 1
        step = fields[k] - fields[i] if k < len(fields) else 1
        while k < len(fields) and fields[k] - fields[k - 1] == step:
            k += 1
        out.append((i, fields[i], step, k - i))
        i = k
    return out


SEL_GROUPS, GAT_GROUPS = grouped(SELECTED, SEL_BANK), grouped(GATHERED, GAT_BANK)
NS = len(SEL_GROUPS)
NG = len(GAT_GROUPS) + 1
GROUPS = NS + NG
EARLY = RING // SEL_BANK
assert GROUPS % 2 == 0 or UNITS % 2 == 0


def pair_row(n, m):
    return n * (2 * FIELDS - 1 - n) // 2 + m - n - 1


W1_LOADS = 1 + sum(((n + 1) % CH > 0) + (-(-(n + 1) // CH) < Q) for n in range(FIELDS - 1))


def bank_of(b, g):
    return (b * GROUPS + g) % 2


def dlrm_tower_kernel(nc, dense_ctx, ids, tables, w1, b1, w2, b2, w3, out):
    chunks = [tables[f].shape[0] // KROWS for f in SELECTED]
    first_chunk = [sum(chunks[:i]) for i in range(N_SEL)]
    most = max(chunks)
    stage_chunks = [(first_chunk[STAGED * g], sum(chunks[STAGED * g:STAGED * (g + 1)])) for g in range(STAGES)]

    with ExitStack() as ctx:
        def sb(name, shape, dt):
            return ctx.enter_context(nc.sbuf_tensor(name, shape, dt))

        def psum(name, shape, dt):
            return ctx.enter_context(nc.psum_tensor(name, shape, dt))

        def sem(name):
            return ctx.enter_context(nc.semaphore(name))

        ident = sb("ident", [P, P], F32)
        row_ids = {c: sb(f"row_ids{c}", [P, c], F32) for c in sorted(set(chunks))}
        ids_all = sb("ids_all", [P, BATCH // P, FIELDS], I32)
        ids_sel = sb("ids_sel", [P, BATCH // P, N_SEL], F32)
        ids_t = sb("ids_t", [N_SEL, BATCH], F16)
        ids_unit = [sb(f"ids_unit{b}", [P, 2, FIELDS], I32) for b in range(2)]
        ctx_unit = [sb(f"ctx_unit{b}", [P, 2, 32], F32) for b in range(2)]
        ids_wide = [sb(f"ids_wide{b}", [P, N_SEL, UNIT], F16) for b in range(2)]
        tabs = sb("tabs", [KROWS, sum(chunks), PARTS, DIM], F32R)
        onehot = [sb(f"onehot{r}", [KROWS, most, UNIT], F32R) for r in range(RING)]
        rows = [sb(f"rows{b}", [P, N_GAT, 2, DIM], F32) for b in range(2)]
        moved = [sb(f"moved{b}", [P, SEL_BANK, P], F32) for b in range(2)]
        vecs = sb("vecs", [P, P, FIELDS], F32)
        prods = sb("prods", [P, CH, UNIT], F32)
        prods_hi = sb("prods_hi", [P, CH, UNIT], F32R)
        prods_lo = sb("prods_lo", [P, CH, UNIT], F32R)
        w1_hi = sb("w1_hi", [P, CH, H1], F32R)
        w1_lo = sb("w1_lo", [P, CH, H1], F32R)
        w2_sb = sb("w2_sb", [P, J1, H2], F32)
        w3_sb = sb("w3_sb", [P, J2], F32)
        b1_sb = sb("b1_sb", [P, J1], F32)
        b2_sb = sb("b2_sb", [P, J2], F32)
        h1 = sb("h1", [P, J1, UNIT], F32)
        h2 = sb("h2", [P, J2, UNIT], F32)
        y = [sb(f"y{b}", [1, UNIT], F32) for b in range(2)]
        w1_stage = vecs[:].rearrange("p s f -> p (s f)").rearrange("p (c j) -> p c j", c=CH)
        stage = prods[0:KROWS].rearrange("p c s -> p (c s)").rearrange("p (k d) -> p k d", d=DIM)

        vecs_ps = psum("vecs_ps", [P, 2, 512], F32)
        prods_ps = psum("prods_ps", [P, ROUNDS, 2, PER_ROUND, FIELDS], F32)
        h1_ps = psum("h1_ps", [P, J1, UNIT], F32)
        h2_ps = prods_ps[:, 0, 0, :, :].rearrange("p i m -> p (i m)").rearrange("p (j s) -> p j s", j=J2)
        y_ps = prods_ps[0:1, 0, 1, 0:UNIT // FIELDS, :].rearrange("p i m -> p (i m)")
        idt_ps = prods_ps[0:N_SEL].rearrange("p r h i m -> p (r h i m)")

        def sel_bank(bank):
            return vecs_ps[:, bank, :].rearrange("p (k h s) -> p k h s", k=SEL_BANK, h=2)

        def gat_bank(bank):
            return vecs_ps[:, bank, :].rearrange("p (k s) -> p k s", k=GAT_BANK)

        def of_round(t, r):
            return t.rearrange("p c (x i) -> p c x i", i=32)[:, :, :, PER_ROUND * r:PER_ROUND * (r + 1)]

        ids_scratch = nc.dram_tensor("ids_scratch", (N_SEL, BATCH), F16, kind="Internal").ap()

        ids_all_in = sem("ids_all_in")
        ids_in = [sem(f"ids_in{b}") for b in range(2)]
        ctx_in = [sem(f"ctx_in{b}") for b in range(2)]
        wide_in = [sem(f"wide_in{b}") for b in range(2)]
        stage_in = sem("stage_in")
        scratch_out = sem("scratch_out")
        w1_in = sem("w1_in")
        w_in = sem("w_in")
        rows_in = [sem(f"rows_in{b}") for b in range(2)]
        y_out = [sem(f"y_out{b}") for b in range(2)]
        ident_zero = sem("ident_zero")
        ident_ready = sem("ident_ready")
        row_ids_ready = sem("row_ids_ready")
        w1_zero = sem("w1_zero")
        ctx_zero = sem("ctx_zero")
        ids_float = sem("ids_float")
        ids_turned = sem("ids_turned")
        ids_t_ready = sem("ids_t_ready")
        tabs_hi_ready = sem("tabs_hi_ready")
        tabs_ready = sem("tabs_ready")
        w1_hi_ready = sem("w1_hi_ready")
        w1_ready = sem("w1_ready")
        onehot_ready = sem("onehot_ready")
        onehot_used = sem("onehot_used")
        group_full = sem("group_full")
        moved_ready = sem("moved_ready")
        sel_emptied = sem("sel_emptied")
        gat_emptied = sem("gat_emptied")
        gram_full = sem("gram_full")
        prods_step = sem("prods_step")
        hi_ready = sem("hi_ready")
        lo_ready = sem("lo_ready")
        h1_full = sem("h1_full")
        h1_ready = sem("h1_ready")
        h2_full = sem("h2_full")
        h2_ready = sem("h2_ready")
        y_full = sem("y_full")
        y_free = sem("y_free")
        y_ready = sem("y_ready")
        passed = {e: sem(f"passed_{e}") for e in ("pe", "pool", "sp")}

        block = ctx.enter_context(nc.Block())

        @block.sync
        def _(sp):
            def load_unit(n, b):
                sp.dma_start(ids_unit[b][:], ids[bass.ds(n * UNIT, UNIT), :].rearrange("(h p) f -> p h f", p=P))\
                  .then_inc(ids_in[b], 16)
                sp.dma_start(ctx_unit[b][:, :, 0:CTX],
                             dense_ctx[bass.ds(n * UNIT, UNIT), :].rearrange("(h p) f -> p h f", p=P))\
                  .then_inc(ctx_in[b], 16)

            def load_wide(n, b):
                sp.dma_start(ids_wide[b][:], ids_scratch[:, bass.ds(n * UNIT, UNIT)].partition_broadcast(P))\
                  .then_inc(wide_in[b], 16)

            def load_stage(g):
                for k in range(STAGED * g, STAGED * (g + 1)):
                    at = first_chunk[k] - stage_chunks[g][0]
                    sp.dma_start(stage[:, at:at + chunks[k], :],
                                 tables[SELECTED[k]].rearrange("(p c) d -> p c d", c=chunks[k])).then_inc(stage_in, 16)

            def load_w1(n):
                q = (n + 1) // CH
                m = n + 1
                if m % CH:
                    sp.dma_start(w1_stage[32 * q + n:32 * q + n + 1, m - CH * q:CH, :],
                                 w1[pair_row(n, m):pair_row(n, m) + CH * (q + 1) - m, :]
                                 .rearrange("(a k) j -> a k j", a=1)).then_inc(w1_in, 16)
                    q += 1
                if q < Q:
                    m = CH * q
                    sp.dma_start(w1_stage[32 * q + n:P:32, :, :],
                                 w1[pair_row(n, m):pair_row(n, m) + CH * (Q - q), :]
                                 .rearrange("(q k) j -> q k j", k=CH)).then_inc(w1_in, 16)

            sp.sem_inc(y_free, 2)
            sp.wait_ge(ctx_zero, 2)
            load_unit(0, 0)
            sp.dma_start(ids_all[:], ids.rearrange("(t p) f -> p t f", p=P)).then_inc(ids_all_in, 16)
            load_stage(0)
            load_unit(1, 1)
            sp.wait_ge(w1_zero, 1)
            sp.dma_start(w1_stage[0:CTX, 0, :], w1[FIELDS * (FIELDS - 1) // 2:, :]).then_inc(w1_in, 16)
            sp.wait_ge(ids_t_ready, 1)
            sp.dma_start(ids_scratch, ids_t[:]).then_inc(scratch_out, 16)
            sp.wait_ge(tabs_ready, 1)
            load_stage(1)
            sp.wait_ge(scratch_out, 16)
            load_wide(0, 0)
            load_wide(1, 1)
            for n in range(8):
                load_w1(n)
            for g in range(2, STAGES):
                sp.wait_ge(tabs_ready, g)
                load_stage(g)
            for n in range(8, FIELDS - 1):
                load_w1(n)
            sp.dma_start(b1_sb[:], b1.rearrange("(c p) -> p c", p=P), allow_slow_non_contiguous=True)\
              .then_inc(w_in, 16)
            sp.dma_start(b2_sb[:], b2.rearrange("(c p) -> p c", p=P), allow_slow_non_contiguous=True)\
              .then_inc(w_in, 16)
            sp.dma_start(w3_sb[:], w3.rearrange("(c p) a -> p (c a)", p=P), allow_slow_non_contiguous=True)\
              .then_inc(w_in, 16)
            sp.dma_start(w2_sb[:], w2.rearrange("(c p) j -> p c j", p=P)).then_inc(w_in, 16)

            def step(n, i, b, more):
                if more:
                    sp.wait_ge(rows_in[b], 16 * 2 * N_GAT * (i + 1))
                    sp.sem_inc(passed["sp"], 1)
                    sp.wait_ge(group_full, GROUPS * (n + 1))
                    sp.sem_inc(passed["sp"], 1)
                    load_unit(n + 2, b)
                    sp.wait_ge(onehot_ready, N_SEL * (n + 1))
                    sp.sem_inc(passed["sp"], 1)
                    load_wide(n + 2, b)
                sp.wait_ge(y_ready, n + 2)
                sp.sem_inc(passed["sp"], 1)
                sp.dma_start(out[bass.ds(n * UNIT, UNIT), :].rearrange("s a -> a s"), y[b][:]).then_inc(y_out[b], 16)
                sp.wait_ge(y_out[b], 16 * (i + 1))
                sp.sem_inc(y_free, 1)

            with sp.Fori(0, UNITS // 2 - 1) as i:
                for b in range(2):
                    step(2 * i + b, i, b, True)
            for b in range(2):
                step(UNITS - 2 + b, UNITS // 2 - 1, b, False)

        @block.gpsimd
        def _(pool):
            nc.gpsimd.memset(ident[:], 0.0).then_inc(ident_zero, 1)
            pool.wait_ge(ident_zero, 1)
            nc.gpsimd.affine_select(out=ident[:], in_=ident[:], compare_op=ALU.not_equal, fill=1.0, base=0,
                                    pattern=[[-1, P]], channel_multiplier=1).then_inc(ident_ready, 1)
            for c, t in row_ids.items():
                nc.gpsimd.iota(t[:], pattern=[[1, c]], base=0, channel_multiplier=c,
                               allow_small_or_imprecise_dtypes=True).then_inc(row_ids_ready, 1)
            with pool.Fori(0, UNITS // 2) as i:
                for b in range(2):
                    pool.wait_ge(ids_in[b], 16 * (i + 1))
                    pool.wait_ge(hi_ready, ROUNDS * (2 * i + b + 1))
                    pool.sem_inc(passed["pool"], 1)
                    for k, f in enumerate(GATHERED):
                        for h in range(2):
                            nc.gpsimd.indirect_dma_start(
                                out=rows[b][:, k, h, :], out_offset=None, in_=tables[f],
                                in_offset=bass.IndirectOffsetOnAxis(ap=ids_unit[b][:, h, f:f + 1], axis=0))\
                              .then_inc(rows_in[b], 16)

        @block.scalar
        def _(act):
            act.sem_inc(hi_ready, 2 * ROUNDS)
            act.sem_inc(gat_emptied, NG)

            def gathered(n, b):
                for g, fields in enumerate(GAT_GROUPS):
                    act.wait_ge(group_full, GROUPS * n + NS + g + 1)
                    bank = gat_bank(bank_of(b, NS + g))
                    for at, f, step_, count in runs(fields):
                        last = nc.scalar.copy(
                            vecs[:, :, f:f + step_ * (count - 1) + 1:step_].rearrange("p s f -> p f s"),
                            bank[:, at:at + count, :])
                    last.then_inc(gat_emptied, 1)

            def move(n, g, b):
                act.wait_ge(group_full, GROUPS * n + g + 1)
                bank = bank_of(b, g)
                nc.scalar.copy(moved[bank][0:DIM], sel_bank(bank)[DIM:P, :, 0, :])
                nc.scalar.copy(moved[bank][DIM:P], sel_bank(bank)[0:DIM, :, 1, :]).then_inc(moved_ready, 1)

            def products(n, r, s):
                if s == 0:
                    act.wait_ge(gram_full, ROUNDS * n + r + 1)
                for q in range(Q):
                    c0 = 1 if q == 0 else 0
                    nc.scalar.copy(
                        of_round(prods[32 * q:32 * q + 32, c0:CH, :], r)
                        .rearrange("p c (h s) i -> p h s i c", h=2)[:, :, s],
                        prods_ps[32 * s:32 * s + 32, r, :, :, CH * q + c0:CH * q + CH])\
                      .then_inc(prods_step, 1)

            def high(n, r):
                act.wait_ge(prods_step, Q * Q * (ROUNDS * n + r + 1))
                nc.scalar.copy(of_round(prods_hi[:], r), of_round(prods[:], r)).then_inc(hi_ready, 1)

            def step(n, b, more):
                gathered(n, b)
                act.wait_ge(group_full, GROUPS * (n + 1))
                act.wait_ge(lo_ready, ROUNDS * (n + 1))
                bank = bank_of(b, GROUPS - 1)
                nc.scalar.copy(prods[0:32, 0, :], vecs_ps[0:32, bank, 0:UNIT]).then_inc(gat_emptied, 1)
                for s in range(Q):
                    products(n, 0, s)
                high(n, 0)
                if more:
                    for g in range(EARLY):
                        move(n + 1, g, 1 - b)
                for s in range(Q):
                    products(n, 1, s)
                    if more and EARLY + s < NS:
                        move(n + 1, EARLY + s, 1 - b)
                high(n, 1)
                if more:
                    for g in range(EARLY + Q, NS):
                        move(n + 1, g, 1 - b)

            for g in range(STAGES):
                act.wait_ge(stage_in, 16 * STAGED * (g + 1))
                c0, k = stage_chunks[g]
                nc.scalar.copy(tabs[:, c0:c0 + k, 0, :], stage[:, 0:k, :]).then_inc(tabs_hi_ready, 1)
            for g in range(EARLY):
                move(0, g, 0)
            act.wait_ge(w1_in, 16 * W1_LOADS)
            nc.scalar.copy(w1_hi[:], w1_stage).then_inc(w1_hi_ready, 1)
            for g in range(EARLY, NS):
                move(0, g, 0)
            with act.Fori(0, UNITS // 2 - 1) as i:
                for b in range(2):
                    step(2 * i + b, b, True)
            step(UNITS - 2, 0, True)
            step(UNITS - 1, 1, False)

        @block.vector
        def _(dve):
            dve.sem_inc(y_ready, 1)
            dve.sem_inc(lo_ready, ROUNDS)
            for b in range(2):
                nc.vector.memset(ctx_unit[b][:], 0.0).then_inc(ctx_zero, 1)
            nc.vector.memset(w1_stage, 0.0).then_inc(w1_zero, 1)
            dve.wait_ge(ids_all_in, 16)
            for at, f, step_, count in runs(SELECTED):
                last = nc.vector.tensor_copy(ids_sel[:, :, at:at + count],
                                             ids_all[:, :, f:f + step_ * (count - 1) + 1:step_])
            last.then_inc(ids_float, 1)

            def low_tables(g):
                c0, k = stage_chunks[g]
                dve.wait_ge(tabs_hi_ready, g + 1)
                nc.vector.tensor_tensor(tabs[:, c0:c0 + k, 1, :], stage[:, 0:k, :],
                                        tabs[:, c0:c0 + k, 0, :].bitcast(F32), ALU.subtract).then_inc(tabs_ready, 1)

            def one_hot(n, k, b):
                before = k - RING if k >= RING else (N_SEL - 1 - (N_SEL - 1 - k) % RING) - N_SEL
                dve.wait_ge(onehot_used, N_SEL * (n + 1) + before + 1)
                for c in range(chunks[k]):
                    last = nc.vector.tensor_scalar(onehot[k % RING][:, c, :], ids_wide[b][0:KROWS, k, :],
                                                   row_ids[chunks[k]][0:KROWS, c:c + 1], None, ALU.is_equal)
                last.then_inc(onehot_ready, 1)

            def one_hots(n, ks, b):
                for k in ks:
                    one_hot(n, k, b)

            def add(n, g, b):
                dve.wait_ge(moved_ready, NS * n + g + 1)
                bank = bank_of(b, g)
                (_, f, step_, count), = runs(SEL_GROUPS[g])
                for h in range(2):
                    half = slice(DIM * h, DIM * h + DIM)
                    last = nc.vector.tensor_tensor(
                        vecs[half, :, f:f + step_ * (count - 1) + 1:step_].rearrange("p s f -> p f s"),
                        sel_bank(bank)[half, :, h, :], moved[bank][half], ALU.add)
                last.then_inc(sel_emptied, 1)

            def low(n, r):
                dve.wait_ge(hi_ready, ROUNDS * (n + 2) + r + 1)
                nc.vector.tensor_tensor(of_round(prods_lo[:], r), of_round(prods[:], r),
                                        of_round(prods_hi[:].bitcast(F32), r), ALU.subtract).then_inc(lo_ready, 1)

            def mlp(n, b):
                for j in range(J1):
                    if j % 2 == 0:
                        dve.wait_ge(h1_full, 2 * n + j // 2 + 1)
                    nc.vector.tensor_scalar(h1[:, j, :], h1_ps[:, j, :], b1_sb[:, j:j + 1], 0.0, ALU.add,
                                            ALU.max).then_inc(h1_ready, 1)
                dve.wait_ge(h2_full, n + 1)
                for j in range(J2):
                    nc.vector.tensor_scalar(h2[:, j, :], h2_ps[:, j, :], b2_sb[:, j:j + 1], 0.0, ALU.add,
                                            ALU.max).then_inc(h2_ready, 1)
                dve.wait_ge(y_full, n + 1)
                dve.wait_ge(y_free, n + 1)
                nc.vector.tensor_copy(y[b][:], y_ps).then_inc(y_ready, 1)

            def rest(n, b):
                for g in range(EARLY, NS):
                    if g + EARLY < NS:
                        one_hots(n, range(SEL_BANK * (g + EARLY), SEL_BANK * (g + EARLY + 1)), b)
                    add(n, g, b)

            def step(n, i, b):
                one_hots(n + 1, range(RING), 1 - b)
                low(n, 0)
                one_hots(n + 1, range(RING, 2 * RING), 1 - b)
                dve.wait_ge(gram_full, ROUNDS * (n + 1))
                for g in range(EARLY):
                    add(n + 1, g, 1 - b)
                for g in range(EARLY, NS):
                    if g + EARLY < NS:
                        one_hots(n + 1, range(SEL_BANK * (g + EARLY), SEL_BANK * (g + EARLY + 1)), 1 - b)
                        add(n + 1, g, 1 - b)
                low(n, 1)
                for g in range(NS - EARLY, NS):
                    add(n + 1, g, 1 - b)
                mlp(n, b)

            low_tables(0)
            dve.wait_ge(ids_turned, 1)
            nc.vector.tensor_copy(ids_t[:], idt_ps).then_inc(ids_t_ready, 1)
            for g in range(1, STAGES):
                low_tables(g)
            dve.wait_ge(row_ids_ready, len(row_ids))
            dve.wait_ge(wide_in[0], 16)
            one_hots(0, range(2 * RING), 0)
            dve.wait_ge(w1_hi_ready, 1)
            nc.vector.tensor_tensor(w1_lo[:], w1_stage, w1_hi[:].bitcast(F32), ALU.subtract).then_inc(w1_ready, 1)
            dve.wait_ge(w1_ready, 1)
            for g in range(EARLY):
                add(0, g, 0)
            rest(0, 0)
            dve.wait_ge(w_in, 16 * 4)
            with dve.Fori(0, UNITS // 2 - 1) as i:
                dve.wait_ge(wide_in[1], 16 * (i + 1))
                step(2 * i, i, 0)
                dve.wait_ge(wide_in[0], 16 * (i + 2))
                step(2 * i + 1, i, 1)
            last_i = UNITS // 2 - 1
            dve.wait_ge(wide_in[1], 16 * (last_i + 1))
            step(UNITS - 2, last_i, 0)
            for r in range(ROUNDS):
                low(UNITS - 1, r)
            mlp(UNITS - 1, 1)

        @block.tensor
        def _(pe):
            pe.sem_inc(onehot_used, N_SEL)

            def select(n, groups, b):
                for g in groups:
                    if g < 2:
                        pe.wait_ge(gat_emptied, NG * (n + 1) - 1 + g)
                    else:
                        pe.wait_ge(sel_emptied, NS * n + g - 1)
                    for at in range(SEL_BANK):
                        k = SEL_BANK * g + at
                        pe.wait_ge(onehot_ready, N_SEL * n + k + 1)
                        for c in range(chunks[k]):
                            last = nc.tensor.matmul(
                                vecs_ps[:, bank_of(b, g), UNIT * at:UNIT * (at + 1)],
                                tabs[:, first_chunk[k] + c, :, :].rearrange("p a d -> p (a d)"),
                                onehot[k % RING][:, c, :], start=(c == 0), stop=(c == chunks[k] - 1),
                                skip_group_check=True)
                        if at < SEL_BANK - 1:
                            last.then_inc(onehot_used, 1)
                        else:
                            last.then_inc(group_full, 1)
                    pe.wait_ge(group_full, GROUPS * n + g + 1)
                    pe.sem_inc(onehot_used, 1)

            def turn(n, i, b):
                pe.wait_ge(rows_in[b], 16 * 2 * N_GAT * (i + 1))
                for x in range(NG):
                    if x < 2:
                        pe.wait_ge(sel_emptied, NS * (n + 1) - 1 + x)
                    else:
                        pe.wait_ge(gat_emptied, NG * (n + 1) + x - 1)
                    bank = bank_of(b, NS + x)
                    if x == NG - 1:
                        pe.wait_ge(ctx_in[b], 16 * (i + 1))
                        for h in range(2):
                            last = nc.tensor.transpose(gat_bank(bank)[0:32, h, :], ctx_unit[b][:, h, :], ident[:])
                    else:
                        for at in range(len(GAT_GROUPS[x])):
                            last = nc.tensor.transpose(
                                gat_bank(bank)[:, at, :],
                                rows[b][:, GAT_BANK * x + at, :, :].rearrange("p h d -> p (h d)"), ident[:])
                    last.then_inc(group_full, 1)

            def gram(n, r):
                if r == 0:
                    pe.wait_ge(gat_emptied, NG * (n + 2))
                    pe.wait_ge(sel_emptied, NS * (n + 1))
                    pe.wait_ge(y_ready, n + 1)
                    pe.sem_inc(passed["pe"], 1)
                for i in range(PER_ROUND):
                    for h in range(2):
                        for s in range(Q):
                            v = vecs[DIM * h:DIM * h + DIM, 32 * s + PER_ROUND * r + i, :]
                            last = nc.tensor.matmul(prods_ps[32 * s:32 * s + 32, r, h, i, :], v, v, start=True, stop=True,
                                                    skip_group_check=True)
                last.then_inc(gram_full, 1)

            def mlp(n):
                pe.wait_ge(lo_ready, ROUNDS * (n + 2))
                for j in range(J1):
                    block_j = slice(P * j, P * j + P)
                    for c in range(CH):
                        terms = ((w1_hi, prods_hi), (w1_hi, prods_lo), (w1_lo, prods_hi))
                        for t, (w, z) in enumerate(terms):
                            last = nc.tensor.matmul(h1_ps[:, j, :], w[:, c, block_j], z[:, c, :],
                                                    start=(c == 0 and t == 0),
                                                    stop=(c == CH - 1 and t == len(terms) - 1))
                    if j % 2 == 1:
                        last.then_inc(h1_full, 1)
                for j in range(J1):
                    pe.wait_ge(h1_ready, J1 * n + j + 1)
                    for o in range(J2):
                        last = nc.tensor.matmul(h2_ps[:, o, :], w2_sb[:, j, P * o:P * o + P], h1[:, j, :],
                                                start=(j == 0 and o == 0), stop=(j == J1 - 1), skip_group_check=True)
                last.then_inc(h2_full, 1)
                for o in range(J2):
                    pe.wait_ge(h2_ready, J2 * n + o + 1)
                    last = nc.tensor.matmul(y_ps, w3_sb[:, o:o + 1], h2[:, o, :], start=(o == 0), stop=(o == J2 - 1))
                last.then_inc(y_full, 1)

            pe.wait_ge(ident_ready, 1)
            pe.wait_ge(ids_float, 1)
            for t in range(BATCH // P):
                last = nc.tensor.transpose(idt_ps[:, P * t:P * t + P], ids_sel[:, t, :], ident[:])
            last.then_inc(ids_turned, 1)
            pe.wait_ge(tabs_ready, STAGES)
            select(0, range(NS), 0)
            pe.wait_ge(ids_t_ready, 1)
            pe.wait_ge(w1_ready, 1)
            pe.wait_ge(w_in, 16 * 4)

            def step(n, i, b):
                turn(n, i, b)
                gram(n, 0)
                select(n + 1, range(EARLY), 1 - b)
                gram(n, 1)
                select(n + 1, range(EARLY, NS), 1 - b)
                mlp(n)

            with pe.Fori(0, UNITS // 2 - 1) as i:
                for b in range(2):
                    step(2 * i + b, i, b)
            last_i = UNITS // 2 - 1
            step(UNITS - 2, last_i, 0)
            turn(UNITS - 1, last_i, 1)
            for r in range(ROUNDS):
                gram(UNITS - 1, r)
            mlp(UNITS - 1)


_INS = ["dense_ctx", "ids"] + [f"tbl_{f}" for f in range(FIELDS)] + ["W_top1", "b_top1", "W_top2", "b_top2", "W_top3"]


def kernel(**inputs):
    import numpy as _np
    import concourse.bacc as _bacc
    from concourse import mybir as _mybir
    from concourse.bass_utils import run_bass_kernel_spmd as _run

    nc = _bacc.Bacc("TRN2", target_bir_lowering=False, num_devices=1)
    arrays, args = {}, {}
    for name in _INS:
        a = _np.ascontiguousarray(inputs[name])
        arrays[f"in_{name}_dram"] = a
        args[name] = nc.dram_tensor(f"in_{name}_dram", a.shape, _mybir.dt.from_np(a.dtype), kind="ExternalInput").ap()
    out = nc.dram_tensor("out_0_dram", (BATCH, 1), _mybir.dt.float32, kind="ExternalOutput").ap()
    dlrm_tower_kernel(nc, args["dense_ctx"], args["ids"], [args[f"tbl_{f}"] for f in range(FIELDS)], args["W_top1"],
                      args["b_top1"], args["W_top2"], args["b_top2"], args["W_top3"], out)
    r = _run(nc, [arrays], core_ids=[0])
    return r.results[0]["out_0_dram"]
```

```python
from contextlib import ExitStack
from itertools import chain, islice

import concourse.bass as bass
from concourse import mybir

F32 = mybir.dt.float32
F32R = mybir.dt.float32r
F16 = mybir.dt.float16
I32 = mybir.dt.int32
ALU = mybir.AluOpType
ACT = mybir.ActivationFunctionType

BATCH, FIELDS, DIM, CTX = 2048, 32, 64, 16
P = 128
UNIT = 2 * P
UNITS = BATCH // UNIT
SELECTED = [7, 8, 9, 11, 12, 15, 17, 18, 20, 22, 24, 25]
GATHERED = [f for f in range(FIELDS) if f not in SELECTED]
N_SEL, N_GAT = len(SELECTED), len(GATHERED)
KROWS = 125
PARTS = 2
RING = 4
SEL_BANK = 2
STAGES = N_SEL // SEL_BANK
GAT_BANK = 4
Q = 4
CH = FIELDS // Q
ROUNDS = 2
PER_ROUND = 32 // ROUNDS
H1, H2 = 512, 256
J1, J2 = H1 // P, H2 // P


def grouped(fields, size):
    return [fields[i:i + size] for i in range(0, len(fields), size)]


def runs(fields):
    out, i = [], 0
    while i < len(fields):
        k = i + 1
        step = fields[k] - fields[i] if k < len(fields) else 1
        while k < len(fields) and fields[k] - fields[k - 1] == step:
            k += 1
        out.append((i, fields[i], step, k - i))
        i = k
    return out


SEL_GROUPS, GAT_GROUPS = grouped(SELECTED, SEL_BANK), grouped(GATHERED, GAT_BANK)
NS = len(SEL_GROUPS)
NG = len(GAT_GROUPS) + 1
GROUPS = NS + NG
AHEAD = RING // SEL_BANK
assert GROUPS % 2 == 0 or UNITS % 2 == 0


def pair_row(n, m):
    return n * (2 * FIELDS - 1 - n) // 2 + m - n - 1


W1_LOADS = 1 + sum(((n + 1) % CH > 0) + (-(-(n + 1) // CH) < Q) for n in range(FIELDS - 1))


def bank_of(b, g):
    return (b * GROUPS + g) % 2


def dlrm_tower_kernel(nc, dense_ctx, ids, tables, w1, b1, w2, b2, w3, out):
    chunks = [tables[f].shape[0] // KROWS for f in SELECTED]
    first_chunk = [sum(chunks[:i]) for i in range(N_SEL)]
    most = max(chunks)
    stage_chunks = [(first_chunk[SEL_BANK * g], sum(chunks[SEL_BANK * g:SEL_BANK * (g + 1)])) for g in range(STAGES)]

    with ExitStack() as ctx:
        def sb(name, shape, dt):
            return ctx.enter_context(nc.sbuf_tensor(name, shape, dt))

        def psum(name, shape, dt):
            return ctx.enter_context(nc.psum_tensor(name, shape, dt))

        def sem(name):
            return ctx.enter_context(nc.semaphore(name))

        ident = sb("ident", [P, P], F32)
        row_ids = {c: sb(f"row_ids{c}", [P, c], F32) for c in sorted(set(chunks))}
        ids_sel = sb("ids_sel", [P, BATCH // P, N_SEL], F32)
        ids_t = sb("ids_t", [N_SEL, BATCH], F16)
        ids_unit = [sb(f"ids_unit{b}", [P, 2, FIELDS], I32) for b in range(2)]
        ctx_unit = [sb(f"ctx_unit{b}", [P, 2, 32], F32) for b in range(2)]
        ids_wide = [sb(f"ids_wide{b}", [P, N_SEL, UNIT], F16) for b in range(2)]
        tabs = sb("tabs", [KROWS, sum(chunks), PARTS, DIM], F32R)
        onehot = [sb(f"onehot{r}", [KROWS, most, UNIT], F32R) for r in range(RING)]
        rows0 = sb("rows0", [P, N_GAT, 2, DIM], F32)
        rows1_prods = sb("rows1_prods", [P, N_GAT * 2 * DIM + CH * UNIT], F32)
        rows = [rows0[:], rows1_prods[:, 0:N_GAT * 2 * DIM].rearrange("p (k h d) -> p k h d", k=N_GAT, h=2)]
        prods = rows1_prods[:, N_GAT * 2 * DIM:].rearrange("p (c s) -> p c s", c=CH)
        moved = [sb(f"moved{b}", [P, SEL_BANK, P], F32) for b in range(2)]
        vecs = sb("vecs", [P, P, FIELDS], F32)
        prods_hi = sb("prods_hi", [P, CH, UNIT], F32R)
        prods_lo = sb("prods_lo", [P, CH, UNIT], F32R)
        w1_hi = sb("w1_hi", [P, CH, H1], F32R)
        w1_lo = sb("w1_lo", [P, CH, H1], F32R)
        w2_sb = sb("w2_sb", [P, J1, H2], F32)
        w3_sb = sb("w3_sb", [P, J2], F32)
        b1_sb = sb("b1_sb", [P, J1], F32)
        b2_sb = sb("b2_sb", [P, J2], F32)
        h1 = sb("h1", [P, J1, UNIT], F32)
        h2_ids = sb("h2_ids", [P, 4 * UNIT], F32)
        h2 = h2_ids[:, 0:J2 * UNIT].rearrange("p (j s) -> p j s", j=J2)
        ids_all = h2_ids[:, J2 * UNIT:].bitcast(I32).rearrange("p (t f) -> p t f", f=FIELDS)
        y = [sb(f"y{b}", [1, UNIT], F32) for b in range(2)]
        w1_stage = rows1_prods[:, 0:CH * H1].rearrange("p (c j) -> p c j", c=CH)
        stage = [h1[0:KROWS].rearrange("p j s -> p (j s)").rearrange("p (k d) -> p k d", d=DIM),
                 h2_ids[0:KROWS].rearrange("p (k d) -> p k d", d=DIM)]
        assert max(k for _, k in stage_chunks) * DIM <= J1 * UNIT

        vecs_ps = psum("vecs_ps", [P, 2, 512], F32)
        prods_ps = psum("prods_ps", [P, ROUNDS, 2, PER_ROUND, FIELDS], F32)
        h1_ps = psum("h1_ps", [P, J1, UNIT], F32)
        h2_ps = prods_ps[:, 0, 0, :, :].rearrange("p i m -> p (i m)").rearrange("p (j s) -> p j s", j=J2)
        y_ps = prods_ps[0:1, 0, 1, 0:UNIT // FIELDS, :].rearrange("p i m -> p (i m)")
        idt_ps = prods_ps[0:N_SEL].rearrange("p r h i m -> p (r h i m)")

        def sel_bank(bank):
            return vecs_ps[:, bank, :].rearrange("p (k h s) -> p k h s", k=SEL_BANK, h=2)

        def gat_bank(bank):
            return vecs_ps[:, bank, :].rearrange("p (k s) -> p k s", k=GAT_BANK)

        def of_round(t, r):
            return t.rearrange("p c (x i) -> p c x i", i=32)[:, :, :, PER_ROUND * r:PER_ROUND * (r + 1)]

        def evacuate(copy, r, s, q):
            c0 = 1 if q == 0 else 0
            return copy(of_round(prods[32 * q:32 * q + 32, c0:CH, :], r)
                        .rearrange("p c (h s) i -> p h s i c", h=2)[:, :, s],
                        prods_ps[32 * s:32 * s + 32, r, :, :, CH * q + c0:CH * q + CH])

        ids_scratch = nc.dram_tensor("ids_scratch", (N_SEL, BATCH), F16, kind="Internal").ap()

        ids_all_in = sem("ids_all_in")
        ids_in = [sem(f"ids_in{b}") for b in range(2)]
        ctx_in = [sem(f"ctx_in{b}") for b in range(2)]
        wide_in = [sem(f"wide_in{b}") for b in range(2)]
        stage_in = [sem(f"stage_in{b}") for b in range(2)]
        scratch_out = sem("scratch_out")
        w1_in = sem("w1_in")
        w_in = sem("w_in")
        rows_in = [sem(f"rows_in{b}") for b in range(2)]
        y_out = [sem(f"y_out{b}") for b in range(2)]
        ident_zero = sem("ident_zero")
        ident_ready = sem("ident_ready")
        row_ids_ready = sem("row_ids_ready")
        w1_zero = sem("w1_zero")
        ctx_zero = sem("ctx_zero")
        ids_float = sem("ids_float")
        ids_turned = sem("ids_turned")
        ids_t_ready = sem("ids_t_ready")
        tabs_hi_ready = sem("tabs_hi_ready")
        tabs_ready = sem("tabs_ready")
        w1_hi_ready = sem("w1_hi_ready")
        w1_ready = sem("w1_ready")
        onehot_ready = sem("onehot_ready")
        first_used = sem("first_used")
        group_full = sem("group_full")
        moved_ready = sem("moved_ready")
        sel_emptied = sem("sel_emptied")
        gat_emptied = sem("gat_emptied")
        gram_full = sem("gram_full")
        prods_step = sem("prods_step")
        dve_step = sem("dve_step")
        hi_ready = sem("hi_ready")
        lo_ready = sem("lo_ready")
        h1_full = sem("h1_full")
        h1_ready = sem("h1_ready")
        h2_full = sem("h2_full")
        h2_ready = sem("h2_ready")
        y_full = sem("y_full")
        y_free = sem("y_free")
        y_ready = sem("y_ready")
        passed = {e: sem(f"passed_{e}") for e in ("pe", "pool", "sp")}

        block = ctx.enter_context(nc.Block())

        @block.sync
        def _(sp):
            def load_unit(n, b):
                sp.dma_start(ids_unit[b][:], ids[bass.ds(n * UNIT, UNIT), :].rearrange("(h p) f -> p h f", p=P))\
                  .then_inc(ids_in[b], 16)
                sp.dma_start(ctx_unit[b][:, :, 0:CTX],
                             dense_ctx[bass.ds(n * UNIT, UNIT), :].rearrange("(h p) f -> p h f", p=P))\
                  .then_inc(ctx_in[b], 16)

            def load_wide(n, b):
                sp.dma_start(ids_wide[b][:], ids_scratch[:, bass.ds(n * UNIT, UNIT)].partition_broadcast(P))\
                  .then_inc(wide_in[b], 16)

            def load_w1(n):
                q = (n + 1) // CH
                m = n + 1
                if m % CH:
                    sp.dma_start(w1_stage[32 * q + n:32 * q + n + 1, m - CH * q:CH, :],
                                 w1[pair_row(n, m):pair_row(n, m) + CH * (q + 1) - m, :]
                                 .rearrange("(a k) j -> a k j", a=1)).then_inc(w1_in, 16)
                    q += 1
                if q < Q:
                    m = CH * q
                    sp.dma_start(w1_stage[32 * q + n:P:32, :, :],
                                 w1[pair_row(n, m):pair_row(n, m) + CH * (Q - q), :]
                                 .rearrange("(q k) j -> q k j", k=CH)).then_inc(w1_in, 16)

            sp.sem_inc(y_free, 2)
            sp.dma_start(ids_all, ids.rearrange("(t p) f -> p t f", p=P)).then_inc(ids_all_in, 16)
            sp.wait_ge(ctx_zero, 2)
            load_unit(0, 0)
            sp.wait_ge(w1_zero, 1)
            sp.dma_start(w1_stage[0:CTX, 0, :], w1[FIELDS * (FIELDS - 1) // 2:, :]).then_inc(w1_in, 16)
            for n in range(FIELDS - 1):
                load_w1(n)
            sp.wait_ge(scratch_out, 16)
            load_wide(1, 1)
            load_unit(1, 1)
            sp.dma_start(b1_sb[:], b1.rearrange("(c p) -> p c", p=P), allow_slow_non_contiguous=True)\
              .then_inc(w_in, 16)
            sp.dma_start(b2_sb[:], b2.rearrange("(c p) -> p c", p=P), allow_slow_non_contiguous=True)\
              .then_inc(w_in, 16)
            sp.dma_start(w3_sb[:], w3.rearrange("(c p) a -> p (c a)", p=P), allow_slow_non_contiguous=True)\
              .then_inc(w_in, 16)
            sp.dma_start(w2_sb[:], w2.rearrange("(c p) j -> p c j", p=P)).then_inc(w_in, 16)

            def load_next(n, i, b):
                sp.wait_ge(rows_in[b], 16 * 2 * N_GAT * (i + 1))
                sp.sem_inc(passed["sp"], 1)
                sp.wait_ge(group_full, GROUPS * (n + 2))
                sp.sem_inc(passed["sp"], 1)
                load_unit(n + 2, b)
                sp.wait_ge(onehot_ready, N_SEL * (n + 1))
                sp.sem_inc(passed["sp"], 1)
                load_wide(n + 2, b)

            def store(n, i, b):
                sp.wait_ge(y_ready, n + 2)
                sp.sem_inc(passed["sp"], 1)
                sp.dma_start(out[bass.ds(n * UNIT, UNIT), :].rearrange("s a -> a s"), y[b][:]).then_inc(y_out[b], 16)
                sp.wait_ge(y_out[b], 16 * (i + 1))
                sp.sem_inc(y_free, 1)

            load_next(0, 0, 0)
            with sp.Fori(0, UNITS // 2 - 2) as i:
                load_next(2 * i + 1, i, 1)
                store(2 * i, i, 0)
                load_next(2 * i + 2, i + 1, 0)
                store(2 * i + 1, i, 1)
            load_next(UNITS - 3, UNITS // 2 - 2, 1)
            for n in range(UNITS - 4, UNITS):
                store(n, n // 2, n % 2)

        @block.gpsimd
        def _(pool):
            nc.gpsimd.memset(w1_stage, 0.0).then_inc(w1_zero, 1)
            nc.gpsimd.memset(ident[:], 0.0).then_inc(ident_zero, 1)
            pool.wait_ge(ident_zero, 1)
            nc.gpsimd.affine_select(out=ident[:], in_=ident[:], compare_op=ALU.not_equal, fill=1.0, base=0,
                                    pattern=[[-1, P]], channel_multiplier=1).then_inc(ident_ready, 1)
            for c, t in row_ids.items():
                nc.gpsimd.iota(t[:], pattern=[[1, c]], base=0, channel_multiplier=c,
                               allow_small_or_imprecise_dtypes=True).then_inc(row_ids_ready, 1)

            def gather(i, b):
                pool.wait_ge(ids_in[b], 16 * (i + 1))
                pool.wait_ge(gat_emptied, NG * (2 * i + b + 1))
                pool.sem_inc(passed["pool"], 1)
                for k, f in enumerate(GATHERED):
                    for h in range(2):
                        nc.gpsimd.indirect_dma_start(
                            out=rows[b][:, k, h, :], out_offset=None, in_=tables[f],
                            in_offset=bass.IndirectOffsetOnAxis(ap=ids_unit[b][:, h, f:f + 1], axis=0))\
                          .then_inc(rows_in[b], 16)

            gather(0, 0)
            pool.wait_ge(w1_ready, 1)
            gather(0, 1)
            with pool.Fori(1, UNITS // 2) as i:
                for b in range(2):
                    gather(i, b)

        @block.scalar
        def _(act):
            act.sem_inc(gat_emptied, 2 * NG)
            act.sem_inc(y_ready, 1)

            def gathered(n, b):
                for g, fields in enumerate(GAT_GROUPS):
                    act.wait_ge(group_full, GROUPS * (n + 1) + NS + g + 1)
                    bank = gat_bank(bank_of(b, NS + g))
                    for at, f, step_, count in runs(fields):
                        last = nc.scalar.copy(
                            vecs[:, :, f:f + step_ * (count - 1) + 1:step_].rearrange("p s f -> p f s"),
                            bank[:, at:at + count, :])
                    last.then_inc(gat_emptied, 1)

            def move(n, g, b):
                act.wait_ge(group_full, GROUPS * (n + 1) + g + 1)
                bank = bank_of(b, g)
                nc.scalar.copy(moved[bank][0:DIM], sel_bank(bank)[DIM:P, :, 0, :])
                nc.scalar.copy(moved[bank][DIM:P], sel_bank(bank)[0:DIM, :, 1, :]).then_inc(moved_ready, 1)

            def products(n, r, s):
                if s == 0:
                    act.wait_ge(gram_full, ROUNDS * n + r + 1)
                for q in range(Q):
                    evacuate(nc.scalar.copy, r, s, q).then_inc(prods_step, 1)

            def high(n):
                act.wait_ge(prods_step, ROUNDS * Q * Q * (n + 1))
                nc.scalar.copy(prods_hi[:], prods).then_inc(hi_ready, 1)

            def layer1(n, half):
                act.wait_ge(h1_full, 2 * n + half + 1)
                for j in range(2 * half, 2 * half + 2):
                    nc.scalar.activation(h1[:, j, :], h1_ps[:, j, :], ACT.Relu, bias=b1_sb[:, j:j + 1])\
                      .then_inc(h1_ready, 1)

            def layers23(n, b):
                act.wait_ge(h2_full, n + 1)
                for j in range(J2):
                    nc.scalar.activation(h2[:, j, :], h2_ps[:, j, :], ACT.Relu, bias=b2_sb[:, j:j + 1])\
                      .then_inc(h2_ready, 1)
                act.wait_ge(y_full, n + 1)
                act.wait_ge(y_free, n + 1)
                nc.scalar.copy(y[b][:], y_ps).then_inc(y_ready, 1)

            def vectors(n, b):
                gathered(n, b)
                act.wait_ge(group_full, GROUPS * (n + 2))
                act.wait_ge(lo_ready, n + 1)
                bank = bank_of(b, GROUPS - 1)
                nc.scalar.copy(prods[0:32, 0, :], vecs_ps[0:32, bank, 0:UNIT]).then_inc(gat_emptied, 1)

            def step(n, b, before):
                vectors(n, b)
                for g in range(2):
                    move(n + 1, g, 1 - b)
                for r in range(ROUNDS):
                    for s in range(Q):
                        products(n, r, s)
                if before:
                    layer1(n - 1, 0)
                for g in range(2, NS - 2):
                    move(n + 1, g, 1 - b)
                if before:
                    layer1(n - 1, 1)
                high(n)
                for g in range(NS - 2, NS):
                    move(n + 1, g, 1 - b)
                if before:
                    layers23(n - 1, 1 - b)

            def load_stage(g):
                for k in range(SEL_BANK * g, SEL_BANK * (g + 1)):
                    at = first_chunk[k] - stage_chunks[g][0]
                    act.dma_start(stage[g % 2][:, at:at + chunks[k], :],
                                  tables[SELECTED[k]].rearrange("(p c) d -> p c d", c=chunks[k]))\
                       .then_inc(stage_in[g % 2], 16)

            def high_tables(g):
                act.wait_ge(stage_in[g % 2], 16 * SEL_BANK * (g // 2 + 1))
                c0, k = stage_chunks[g]
                nc.scalar.copy(tabs[:, c0:c0 + k, 0, :], stage[g % 2][:, 0:k, :]).then_inc(tabs_hi_ready, 1)

            load_stage(0)
            act.wait_ge(ids_float, 1)
            load_stage(1)
            act.wait_ge(ids_turned, 1)
            nc.scalar.copy(ids_t[:, BATCH // 2:], idt_ps[:, BATCH // 2:]).then_inc(ids_t_ready, 1)
            act.wait_ge(ids_t_ready, 2)
            act.dma_start(ids_scratch, ids_t[:]).then_inc(scratch_out, 16)
            for g in range(STAGES):
                high_tables(g)
                if g == 0:
                    act.wait_ge(scratch_out, 16)
                    act.dma_start(ids_wide[0][:], ids_scratch[:, 0:UNIT].partition_broadcast(P))\
                       .then_inc(wide_in[0], 16)
                if g >= 1 and g + 1 < STAGES:
                    act.wait_ge(tabs_ready, g)
                    load_stage(g + 1)
                if g >= STAGES // 2:
                    move(0, g - STAGES // 2, 0)
            act.wait_ge(w1_in, 16 * W1_LOADS)
            nc.scalar.copy(w1_hi[:], w1_stage).then_inc(w1_hi_ready, 1)
            act.wait_ge(w_in, 16 * 4)
            for g in range(STAGES - STAGES // 2, NS):
                move(0, g, 0)
            step(0, 0, False)
            with act.Fori(0, UNITS // 2 - 1) as i:
                step(2 * i + 1, 1, True)
                step(2 * i + 2, 0, True)
            vectors(UNITS - 1, 1)
            for s in range(Q):
                products(UNITS - 1, 0, s)
            for half in range(2):
                layer1(UNITS - 2, half)
            act.wait_ge(prods_step, Q * Q * (ROUNDS * UNITS - 1))
            nc.scalar.copy(of_round(prods_hi, 0), of_round(prods, 0)).then_inc(hi_ready, 1)
            for s in range(Q // 2):
                products(UNITS - 1, 1, s)
            act.wait_ge(prods_step, Q * Q * (ROUNDS * UNITS - 1) + Q * Q // 2)
            act.wait_ge(dve_step, Q * Q // 2)
            nc.scalar.copy(of_round(prods_hi, 1), of_round(prods, 1)).then_inc(hi_ready, 1)
            layers23(UNITS - 2, 0)
            for half in range(2):
                layer1(UNITS - 1, half)
            layers23(UNITS - 1, 1)

        @block.vector
        def _(dve):
            dve.sem_inc(lo_ready, 1)
            for b in range(2):
                nc.vector.memset(ctx_unit[b][:], 0.0).then_inc(ctx_zero, 1)
            dve.wait_ge(ids_all_in, 16)
            for at, f, step_, count in runs(SELECTED):
                last = nc.vector.tensor_copy(ids_sel[:, :, at:at + count],
                                             ids_all[:, :, f:f + step_ * (count - 1) + 1:step_])
            last.then_inc(ids_float, 1)

            def low_tables(g):
                c0, k = stage_chunks[g]
                dve.wait_ge(tabs_hi_ready, g + 1)
                nc.vector.tensor_tensor(tabs[:, c0:c0 + k, 1, :], stage[g % 2][:, 0:k, :],
                                        tabs[:, c0:c0 + k, 0, :].bitcast(F32), ALU.subtract).then_inc(tabs_ready, 1)

            def one_hot(n, k, b):
                before = k - RING if k >= RING else N_SEL - 1 - (N_SEL - 1 - k) % RING
                units, g = (n + 1 if k >= RING else n), before // SEL_BANK
                if before % SEL_BANK == 0:
                    dve.wait_ge(first_used, NS * units + g + 1)
                else:
                    dve.wait_ge(group_full, GROUPS * units + g + 1)
                for c in range(chunks[k]):
                    last = nc.vector.tensor_scalar(onehot[k % RING][:, c, :], ids_wide[b][0:KROWS, k, :],
                                                   row_ids[chunks[k]][0:KROWS, c:c + 1], None, ALU.is_equal)
                last.then_inc(onehot_ready, 1)

            def one_hots(n, ks, b):
                for k in ks:
                    one_hot(n, k, b)

            def add(n, g, b):
                dve.wait_ge(moved_ready, NS * n + g + 1)
                bank = bank_of(b, g)
                (_, f, step_, count), = runs(SEL_GROUPS[g])
                for h in range(2):
                    half = slice(DIM * h, DIM * h + DIM)
                    last = nc.vector.tensor_tensor(
                        vecs[half, :, f:f + step_ * (count - 1) + 1:step_].rearrange("p s f -> p f s"),
                        sel_bank(bank)[half, :, h, :], moved[bank][half], ALU.add)
                last.then_inc(sel_emptied, 1)

            def low(n):
                dve.wait_ge(hi_ready, n + 1)
                nc.vector.tensor_tensor(prods_lo[:], prods, prods_hi[:].bitcast(F32), ALU.subtract)\
                  .then_inc(lo_ready, 1)

            def pair(n, g, b):
                one_hots(n, range(SEL_BANK * g, SEL_BANK * (g + 1)), b)

            def step(n, i1, b):
                dve.wait_ge(wide_in[1 - b], 16 * (i1 + 1))
                for g in range(AHEAD):
                    pair(n + 1, g, 1 - b)
                for g in range(2):
                    pair(n + 1, g + AHEAD, 1 - b)
                dve.wait_ge(gram_full, ROUNDS * (n + 1))
                for g in range(2):
                    add(n + 1, g, 1 - b)
                for g in range(2, NS - AHEAD):
                    pair(n + 1, g + AHEAD, 1 - b)
                    add(n + 1, g, 1 - b)
                low(n)
                for g in range(NS - AHEAD, NS):
                    add(n + 1, g, 1 - b)

            dve.wait_ge(ids_turned, 1)
            nc.vector.tensor_copy(ids_t[:, 0:BATCH // 2], idt_ps[:, 0:BATCH // 2]).then_inc(ids_t_ready, 1)
            for g in range(2):
                low_tables(g)
            dve.wait_ge(row_ids_ready, len(row_ids))
            dve.wait_ge(wide_in[0], 16)
            for g in range(NS):
                pair(0, g, 0)
                if g + 2 < STAGES:
                    low_tables(g + 2)
                if g >= AHEAD:
                    add(0, g - AHEAD, 0)
                if g == NS - 2:
                    dve.wait_ge(w1_hi_ready, 1)
                    nc.vector.tensor_tensor(w1_lo[:], w1_stage, w1_hi[:].bitcast(F32), ALU.subtract)\
                      .then_inc(w1_ready, 1)
            for g in range(NS - AHEAD, NS):
                add(0, g, 0)
            step(0, 0, 0)
            with dve.Fori(0, UNITS // 2 - 1) as i:
                step(2 * i + 1, i + 1, 1)
                step(2 * i + 2, i + 1, 0)
            dve.wait_ge(hi_ready, UNITS)
            nc.vector.tensor_tensor(of_round(prods_lo, 0), of_round(prods, 0), of_round(prods_hi, 0).bitcast(F32),
                                    ALU.subtract).then_inc(lo_ready, 1)
            dve.wait_ge(gram_full, ROUNDS * UNITS)
            for s in range(Q // 2, Q):
                for q in range(Q):
                    evacuate(nc.vector.tensor_copy, 1, s, q).then_inc(dve_step, 1)
            dve.wait_ge(hi_ready, UNITS + 1)
            nc.vector.tensor_tensor(of_round(prods_lo, 1), of_round(prods, 1), of_round(prods_hi, 1).bitcast(F32),
                                    ALU.subtract).then_inc(lo_ready, 1)

        @block.tensor
        def _(pe):
            pe.sem_inc(first_used, NS)
            pe.sem_inc(group_full, GROUPS)

            def take(products, count=None):
                for _ in islice(products, count):
                    pass

            def select_steps(n, groups, b):
                for g in groups:
                    if g < 2:
                        pe.wait_ge(gat_emptied, NG * (n + 2) - 1 + g)
                    else:
                        pe.wait_ge(sel_emptied, NS * n + g - 1)
                    for at in range(SEL_BANK):
                        k = SEL_BANK * g + at
                        pe.wait_ge(onehot_ready, N_SEL * n + k + 1)
                        for c in range(chunks[k]):
                            last = nc.tensor.matmul(
                                vecs_ps[:, bank_of(b, g), UNIT * at:UNIT * (at + 1)],
                                tabs[:, first_chunk[k] + c, :, :].rearrange("p a d -> p (a d)"),
                                onehot[k % RING][:, c, :], start=(c == 0), stop=(c == chunks[k] - 1),
                                skip_group_check=True)
                            if c == chunks[k] - 1:
                                last.then_inc(first_used if at < SEL_BANK - 1 else group_full, 1)
                            yield

            def turn(n, i, b, between, each):
                pe.wait_ge(rows_in[b], 16 * 2 * N_GAT * (i + 1))
                for x in range(NG):
                    if x < 2:
                        pe.wait_ge(sel_emptied, NS * (n + 1) - 1 + x)
                    else:
                        pe.wait_ge(gat_emptied, NG * (n + 2) + x - 1)
                    bank = bank_of(b, NS + x)
                    if x == NG - 1:
                        pe.wait_ge(ctx_in[b], 16 * (i + 1))
                        for h in range(2):
                            last = nc.tensor.transpose(gat_bank(bank)[0:32, h, :], ctx_unit[b][:, h, :], ident[:])
                    else:
                        for at in range(len(GAT_GROUPS[x])):
                            last = nc.tensor.transpose(
                                gat_bank(bank)[:, at, :],
                                rows[b][:, GAT_BANK * x + at, :, :].rearrange("p h d -> p (h d)"), ident[:])
                    last.then_inc(group_full, 1)
                    take(between, each)

            def gram(n, r, between, each):
                if r == 0:
                    pe.wait_ge(gat_emptied, NG * (n + 3))
                    pe.wait_ge(sel_emptied, NS * (n + 1))
                    if not isinstance(n, int) or n > 0:
                        pe.wait_ge(y_ready, n)
                    pe.sem_inc(passed["pe"], 1)
                for i in range(PER_ROUND):
                    for h in range(2):
                        for s in range(Q):
                            v = vecs[DIM * h:DIM * h + DIM, 32 * s + PER_ROUND * r + i, :]
                            last = nc.tensor.matmul(prods_ps[32 * s:32 * s + 32, r, h, i, :], v, v, start=True, stop=True,
                                                    skip_group_check=True)
                    if i == PER_ROUND - 1:
                        last.then_inc(gram_full, 1)
                    take(between, each)

            def layer1_steps(n, half, lows=1):
                if half == 0:
                    pe.wait_ge(lo_ready, n + 1 + lows)
                for j in range(2 * half, 2 * half + 2):
                    block_j = slice(P * j, P * j + P)
                    for c in range(CH):
                        terms = ((w1_hi, prods_hi), (w1_hi, prods_lo), (w1_lo, prods_hi))
                        for t, (w, z) in enumerate(terms):
                            last = nc.tensor.matmul(h1_ps[:, j, :], w[:, c, block_j], z[:, c, :],
                                                    start=(c == 0 and t == 0),
                                                    stop=(c == CH - 1 and t == len(terms) - 1))
                            if j == 2 * half + 1 and c == CH - 1 and t == len(terms) - 1:
                                last.then_inc(h1_full, 1)
                            yield

            def layers23(n, grams):
                pe.wait_ge(prods_step, Q * Q * (ROUNDS * grams - 1))
                for j in range(J1):
                    pe.wait_ge(h1_ready, J1 * n + j + 1)
                    for o in range(J2):
                        last = nc.tensor.matmul(h2_ps[:, o, :], w2_sb[:, j, P * o:P * o + P], h1[:, j, :],
                                                start=(j == 0 and o == 0), stop=(j == J1 - 1), skip_group_check=True)
                last.then_inc(h2_full, 1)
                for o in range(J2):
                    pe.wait_ge(h2_ready, J2 * n + o + 1)
                    last = nc.tensor.matmul(y_ps, w3_sb[:, o:o + 1], h2[:, o, :], start=(o == 0), stop=(o == J2 - 1))
                last.then_inc(y_full, 1)

            pe.wait_ge(ident_ready, 1)
            pe.wait_ge(ids_float, 1)
            for t in range(BATCH // P):
                last = nc.tensor.transpose(idt_ps[:, P * t:P * t + P], ids_sel[:, t, :], ident[:])
            last.then_inc(ids_turned, 1)
            for g in range(NS):
                pe.wait_ge(tabs_ready, g + 1)
                take(select_steps(0, [g], 0))
            pe.wait_ge(ids_t_ready, 2)
            pe.wait_ge(w1_ready, 1)
            pe.wait_ge(w_in, 16 * 4)

            def step(n, i, b, before):
                layer = layer1_steps(n - 1, 0) if before else iter(())
                first = select_steps(n + 1, range(2), 1 - b)
                turn(n, i, b, layer, 2)
                gram(n, 0, first, 2)
                gram(n, 1, layer, 2)
                take(layer)
                take(select_steps(n + 1, range(2, NS - 2), 1 - b))
                if before:
                    take(layer1_steps(n - 1, 1))
                take(select_steps(n + 1, range(NS - 2, NS), 1 - b))
                if before:
                    layers23(n - 1, n + 1)

            step(0, 0, 0, False)
            with pe.Fori(0, UNITS // 2 - 1) as i:
                step(2 * i + 1, i, 1, True)
                step(2 * i + 2, i + 1, 0, True)
            layer = chain(layer1_steps(UNITS - 2, 0), layer1_steps(UNITS - 2, 1))
            turn(UNITS - 1, UNITS // 2 - 1, 1, layer, 4)
            gram(UNITS - 1, 0, layer, 3)
            gram(UNITS - 1, 1, layer, 3)
            layers23(UNITS - 2, UNITS)
            for half in range(2):
                take(layer1_steps(UNITS - 1, half, 2))
            layers23(UNITS - 1, UNITS)


_INS = ["dense_ctx", "ids"] + [f"tbl_{f}" for f in range(FIELDS)] + ["W_top1", "b_top1", "W_top2", "b_top2", "W_top3"]


def kernel(**inputs):
    import numpy as _np
    import concourse.bacc as _bacc
    from concourse import mybir as _mybir
    from concourse.bass_utils import run_bass_kernel_spmd as _run

    nc = _bacc.Bacc("TRN2", target_bir_lowering=False, num_devices=1)
    arrays, args = {}, {}
    for name in _INS:
        a = _np.ascontiguousarray(inputs[name])
        arrays[f"in_{name}_dram"] = a
        args[name] = nc.dram_tensor(f"in_{name}_dram", a.shape, _mybir.dt.from_np(a.dtype), kind="ExternalInput").ap()
    out = nc.dram_tensor("out_0_dram", (BATCH, 1), _mybir.dt.float32, kind="ExternalOutput").ap()
    dlrm_tower_kernel(nc, args["dense_ctx"], args["ids"], [args[f"tbl_{f}"] for f in range(FIELDS)], args["W_top1"],
                      args["b_top1"], args["W_top2"], args["b_top2"], args["W_top3"], out)
    r = _run(nc, [arrays], core_ids=[0])
    return r.results[0]["out_0_dram"]
```
